# Optimizing a Trainium2 kernel written in Bass

```python
import numpy as np
import jax
import jax.numpy as jnp

def _softmax(x, axis=-1):
    return jax.nn.softmax(x, axis=axis)

def _gelu(x):
    return jax.nn.gelu(x, approximate=True)

def _silu(x):
    return jax.nn.silu(x)

def _sigmoid(x):
    return jax.nn.sigmoid(x)

def _layernorm(x, axis=-1, eps=1e-05):
    m = jnp.mean(x, axis=axis, keepdims=True)
    v = jnp.var(x, axis=axis, keepdims=True)
    return (x - m) / jnp.sqrt(v + eps)

def _scatter_add(tgt, idx, src, axis=0):
    return tgt.at[idx].add(src)

def _segment_sum(src, seg, n):
    return jax.ops.segment_sum(src, seg, n)
kernel_name = 'mk_dlrm_tower_d1_rec_r8_cfaab7'

def setup_inputs(seed: int=0):
    np.random.seed(seed)
    _w = jnp.asarray

    def _rec_inputs():
        import jax
        import jax.numpy as jnp
        _tk = jax.random.key(seed)
        ids = jnp.stack([jax.random.randint(jax.random.fold_in(_tk, 200 + f), (512,), 0, v, jnp.int32) for f, v in enumerate([1250, 12500, 1000, 1250, 125000, 1250, 1000, 1250, 12500, 1250, 1250, 1000, 1000, 1250, 12500, 12500, 1000, 12500, 12500, 12500, 12500, 1000, 1000, 1250, 1250, 1000, 1250])], axis=1)
        tbl_0 = 0.05 * jax.random.normal(jax.random.fold_in(_tk, 500 + 0), (1250, 128), jnp.float32)
        tbl_1 = 0.05 * jax.random.normal(jax.random.fold_in(_tk, 500 + 1), (12500, 128), jnp.float32)
        tbl_2 = 0.05 * jax.random.normal(jax.random.fold_in(_tk, 500 + 2), (1000, 128), jnp.float32)
        tbl_3 = 0.05 * jax.random.normal(jax.random.fold_in(_tk, 500 + 3), (1250, 128), jnp.float32)
        tbl_4 = 0.05 * jax.random.normal(jax.random.fold_in(_tk, 500 + 4), (125000, 128), jnp.float32)
        tbl_5 = 0.05 * jax.random.normal(jax.random.fold_in(_tk, 500 + 5), (1250, 128), jnp.float32)
        tbl_6 = 0.05 * jax.random.normal(jax.random.fold_in(_tk, 500 + 6), (1000, 128), jnp.float32)
        tbl_7 = 0.05 * jax.random.normal(jax.random.fold_in(_tk, 500 + 7), (1250, 128), jnp.float32)
        tbl_8 = 0.05 * jax.random.normal(jax.random.fold_in(_tk, 500 + 8), (12500, 128), jnp.float32)
        tbl_9 = 0.05 * jax.random.normal(jax.random.fold_in(_tk, 500 + 9), (1250, 128), jnp.float32)
        tbl_10 = 0.05 * jax.random.normal(jax.random.fold_in(_tk, 500 + 10), (1250, 128), jnp.float32)
        tbl_11 = 0.05 * jax.random.normal(jax.random.fold_in(_tk, 500 + 11), (1000, 128), jnp.float32)
        tbl_12 = 0.05 * jax.random.normal(jax.random.fold_in(_tk, 500 + 12), (1000, 128), jnp.float32)
        tbl_13 = 0.05 * jax.random.normal(jax.random.fold_in(_tk, 500 + 13), (1250, 128), jnp.float32)
        tbl_14 = 0.05 * jax.random.normal(jax.random.fold_in(_tk, 500 + 14), (12500, 128), jnp.float32)
        tbl_15 = 0.05 * jax.random.normal(jax.random.fold_in(_tk, 500 + 15), (12500, 128), jnp.float32)
        tbl_16 = 0.05 * jax.random.normal(jax.random.fold_in(_tk, 500 + 16), (1000, 128), jnp.float32)
        tbl_17 = 0.05 * jax.random.normal(jax.random.fold_in(_tk, 500 + 17), (12500, 128), jnp.float32)
        tbl_18 = 0.05 * jax.random.normal(jax.random.fold_in(_tk, 500 + 18), (12500, 128), jnp.float32)
        tbl_19 = 0.05 * jax.random.normal(jax.random.fold_in(_tk, 500 + 19), (12500, 128), jnp.float32)
        tbl_20 = 0.05 * jax.random.normal(jax.random.fold_in(_tk, 500 + 20), (12500, 128), jnp.float32)
        tbl_21 = 0.05 * jax.random.normal(jax.random.fold_in(_tk, 500 + 21), (1000, 128), jnp.float32)
        tbl_22 = 0.05 * jax.random.normal(jax.random.fold_in(_tk, 500 + 22), (1000, 128), jnp.float32)
        tbl_23 = 0.05 * jax.random.normal(jax.random.fold_in(_tk, 500 + 23), (1250, 128), jnp.float32)
        tbl_24 = 0.05 * jax.random.normal(jax.random.fold_in(_tk, 500 + 24), (1250, 128), jnp.float32)
        tbl_25 = 0.05 * jax.random.normal(jax.random.fold_in(_tk, 500 + 25), (1000, 128), jnp.float32)
        tbl_26 = 0.05 * jax.random.normal(jax.random.fold_in(_tk, 500 + 26), (1250, 128), jnp.float32)
        _rk = jax.random.fold_in(_tk, 7)
        r_bottom_mlp_out = 4.13588e-05 + 0.999923 * jax.random.normal(jax.random.fold_in(_rk, 101), (512, 128), jnp.float32)
        W_top1 = 0.0405887 * jax.random.normal(jax.random.fold_in(_tk, 801), (607, 512), jnp.float32)
        W_top2 = 0.0441942 * jax.random.normal(jax.random.fold_in(_tk, 802), (512, 256), jnp.float32)
        W_top3 = 0.0625 * jax.random.normal(jax.random.fold_in(_tk, 803), (256, 1), jnp.float32)
        b_top1 = jnp.zeros((512,), jnp.float32)
        b_top2 = jnp.zeros((256,), jnp.float32)
        return (r_bottom_mlp_out, ids, tbl_0, tbl_1, tbl_2, tbl_3, tbl_4, tbl_5, tbl_6, tbl_7, tbl_8, tbl_9, tbl_10, tbl_11, tbl_12, tbl_13, tbl_14, tbl_15, tbl_16, tbl_17, tbl_18, tbl_19, tbl_20, tbl_21, tbl_22, tbl_23, tbl_24, tbl_25, tbl_26, W_top1, b_top1, W_top2, b_top2, W_top3)
    r_bottom_mlp_out, ids, tbl_0, tbl_1, tbl_2, tbl_3, tbl_4, tbl_5, tbl_6, tbl_7, tbl_8, tbl_9, tbl_10, tbl_11, tbl_12, tbl_13, tbl_14, tbl_15, tbl_16, tbl_17, tbl_18, tbl_19, tbl_20, tbl_21, tbl_22, tbl_23, tbl_24, tbl_25, tbl_26, W_top1, b_top1, W_top2, b_top2, W_top3 = _rec_inputs()

    def _L0_rec_setup():
        import jax, jax.numpy as jnp
        import numpy as np
        NUM_FEATURES = 27

        def _tril_indices(F):
            idx = []
            for i in range(F):
                for j in range(i):
                    idx.append(i * F + j)
            return np.asarray(idx, dtype=np.int32)
        TRIL_IDX = _tril_indices(NUM_FEATURES)
        key = jax.random.key(seed)
        k1, k2 = jax.random.split(key)
        B, F, D = (8192, NUM_FEATURES, 128)
        features = jax.random.normal(k1, (B, F, D), dtype=jnp.float32)
        bottom_mlp_out = jax.random.normal(k2, (B, D), dtype=jnp.float32)
        return {'features': features, 'bottom_mlp_out': bottom_mlp_out}
    _L0_rec_all = _L0_rec_setup()
    _L0_rec_in = {k: v for k, v in _L0_rec_all.items() if k in ()}
    del _L0_rec_all
    return {'r_bottom_mlp_out': r_bottom_mlp_out, 'ids': ids, 'tbl_0': tbl_0, 'tbl_1': tbl_1, 'tbl_2': tbl_2, 'tbl_3': tbl_3, 'tbl_4': tbl_4, 'tbl_5': tbl_5, 'tbl_6': tbl_6, 'tbl_7': tbl_7, 'tbl_8': tbl_8, 'tbl_9': tbl_9, 'tbl_10': tbl_10, 'tbl_11': tbl_11, 'tbl_12': tbl_12, 'tbl_13': tbl_13, 'tbl_14': tbl_14, 'tbl_15': tbl_15, 'tbl_16': tbl_16, 'tbl_17': tbl_17, 'tbl_18': tbl_18, 'tbl_19': tbl_19, 'tbl_20': tbl_20, 'tbl_21': tbl_21, 'tbl_22': tbl_22, 'tbl_23': tbl_23, 'tbl_24': tbl_24, 'tbl_25': tbl_25, 'tbl_26': tbl_26, 'W_top1': W_top1, 'b_top1': b_top1, 'W_top2': W_top2, 'b_top2': b_top2, 'W_top3': W_top3}

def reference(r_bottom_mlp_out, ids, tbl_0, tbl_1, tbl_2, tbl_3, tbl_4, tbl_5, tbl_6, tbl_7, tbl_8, tbl_9, tbl_10, tbl_11, tbl_12, tbl_13, tbl_14, tbl_15, tbl_16, tbl_17, tbl_18, tbl_19, tbl_20, tbl_21, tbl_22, tbl_23, tbl_24, tbl_25, tbl_26, W_top1, b_top1, W_top2, b_top2, W_top3):
    import jax
    import jax.numpy as jnp

    def _L0_rec_ref(features, bottom_mlp_out):
        import jax, jax.numpy as jnp
        import numpy as np
        NUM_FEATURES = 27

        def _tril_indices(F):
            idx = []
            for i in range(F):
                for j in range(i):
                    idx.append(i * F + j)
            return np.asarray(idx, dtype=np.int32)
        TRIL_IDX = _tril_indices(NUM_FEATURES)
        B = features.shape[0]
        F = features.shape[1]
        interactions = jnp.einsum('bfd,bgd->bfg', features, features)
        interactions = interactions.reshape(B, F * F)
        x = interactions[:, TRIL_IDX]
        return jnp.concatenate([bottom_mlp_out, x], axis=1)
    e = jnp.stack([tbl_0[ids[:, 0]], tbl_1[ids[:, 1]], tbl_2[ids[:, 2]], tbl_3[ids[:, 3]], tbl_4[ids[:, 4]], tbl_5[ids[:, 5]], tbl_6[ids[:, 6]], tbl_7[ids[:, 7]], tbl_8[ids[:, 8]], tbl_9[ids[:, 9]], tbl_10[ids[:, 10]], tbl_11[ids[:, 11]], tbl_12[ids[:, 12]], tbl_13[ids[:, 13]], tbl_14[ids[:, 14]], tbl_15[ids[:, 15]], tbl_16[ids[:, 16]], tbl_17[ids[:, 17]], tbl_18[ids[:, 18]], tbl_19[ids[:, 19]], tbl_20[ids[:, 20]], tbl_21[ids[:, 21]], tbl_22[ids[:, 22]], tbl_23[ids[:, 23]], tbl_24[ids[:, 24]], tbl_25[ids[:, 25]], tbl_26[ids[:, 26]]], axis=1)
    z = _L0_rec_ref(e, r_bottom_mlp_out)
    z = z.reshape(z.shape[0], -1)
    h = jnp.concatenate([z, r_bottom_mlp_out], axis=1)
    h = jnp.maximum(h @ W_top1 + b_top1, 0.0)
    h = jnp.maximum(h @ W_top2 + b_top2, 0.0)
    y = h @ W_top3
    return y

_drawn_inputs = setup_inputs


def setup_inputs(seed=0):
    import zlib

    import numpy as np

    out = dict(_drawn_inputs(seed))
    spreads = {'b_top1': (0.0, 0.1), 'b_top2': (0.0, 0.1)}
    factors = {'tbl_0': 4.636,
     'tbl_1': 5.155,
     'tbl_2': 4.693,
     'tbl_3': 4.034,
     'tbl_4': 4.92,
     'tbl_5': 4.232,
     'tbl_6': 4.568,
     'tbl_7': 4.024,
     'tbl_8': 4.672,
     'tbl_9': 5.051,
     'tbl_10': 4.381,
     'tbl_11': 4.426,
     'tbl_12': 4.664,
     'tbl_13': 4.373,
     'tbl_14': 5.005,
     'tbl_15': 4.818,
     'tbl_16': 4.81,
     'tbl_17': 5.366,
     'tbl_18': 4.16,
     'tbl_19': 4.139,
     'tbl_20': 4.148,
     'tbl_21': 5.054,
     'tbl_22': 4.934,
     'tbl_23': 4.78,
     'tbl_24': 4.363,
     'tbl_25': 5.126,
     'tbl_26': 4.566}
    for name, (base, spread) in spreads.items():
        noise = np.random.default_rng([zlib.crc32(name.encode()), seed]).standard_normal(out[name].shape)
        drawn = base * np.exp(spread * noise) if base else spread * noise
        out[name] = jnp.asarray(drawn.astype(out[name].dtype))
    for name, factor in factors.items():
        out[name] = (out[name] * factor).astype(out[name].dtype)
    return out
```

```python
from contextlib import ExitStack

import concourse.bass as bass
from concourse import mybir

F = 27
D = 128
B = 512
FP = 32
QUADS = 128 // FP
CHUNKS = -(-F // QUADS)
PAIRS = F * (F - 1) // 2
N1, N2 = 512, 256
NT1, NT2 = N1 // 128, N2 // 128
TILES = [128, 128, 128, 128]
SPAN = 8
BATCH = SPAN * QUADS
TRG = 4
TRS = -(-F // TRG)
MAXT = max(TILES)


def build(nc, bottom, ids, tables, w1p, w1b, w2, b2, w3, out):
    fp32, i32 = mybir.dt.float32, mybir.dt.int32
    ALU = mybir.AluOpType
    ACT = mybir.ActivationFunctionType
    starts = [sum(TILES[:t]) for t in range(len(TILES))]
    batches = [n // BATCH for n in TILES]
    first_batch = [sum(batches[:t]) for t in range(len(TILES))]

    with ExitStack() as ctx:
        def sb(name, shape, dt=fp32):
            return ctx.enter_context(nc.sbuf_tensor(name, shape, dt))

        def ps(name, shape):
            return ctx.enter_context(nc.psum_tensor(name, shape, fp32))

        def sem(name):
            return ctx.enter_context(nc.semaphore(name))

        ids_sb = sb("ids_sb", [128, len(TILES), F], i32)
        gathered_sb = sb("gathered_sb", [128, 2, F, D])
        turned = sb("turned", [D, MAXT, FP])
        pairs = sb("pairs", [128, CHUNKS, MAXT])
        bottom_sb = sb("bottom_sb", [128, B // 128, D])
        bottom_t = sb("bottom_t", [D, B])
        ident = sb("ident", [128, 128])
        w1p_sb = sb("w1p_sb", [128, CHUNKS, N1])
        w1b_sb = sb("w1b_sb", [D, 2, N1])
        w1s = sb("w1s", [D, N1])
        w2_sb = sb("w2_sb", [128, NT1, N2])
        b2_sb = sb("b2_sb", [128, NT2])
        w3_sb = sb("w3_sb", [128, NT2])
        h1 = sb("h1", [128, NT1, MAXT])
        h2 = sb("h2", [128, NT2, MAXT])
        y_sb = sb("y_sb", [1, B])

        turn_ps = ps("turn_ps", [128, 2, TRG, 128])
        prod_ps = ps("prod_ps", [128, 2, SPAN, 128])
        h1_ps = ps("h1_ps", [128, 512])
        h2_ps = ps("h2_ps", [128, 512])

        ids_loaded = sem("ids_loaded")
        bottom_loaded = sem("bottom_loaded")
        w1p_loaded = sem("w1p_loaded")
        w1b_loaded = sem("w1b_loaded")
        w2_loaded = sem("w2_loaded")
        small_loaded = sem("small_loaded")
        gathered = [[sem(f"gathered_{p}_{j}") for j in range(TRS)] for p in range(2)]
        ident_zeroed = sem("ident_zeroed")
        ident_made = sem("ident_made")
        pads_set = sem("pads_set")
        bottom_turned = sem("bottom_turned")
        bottom_copied = sem("bottom_copied")
        w1s_made = sem("w1s_made")
        turned_ready = sem("turned_ready")
        turn_copied = [sem("turn_copied_dve"), sem("turn_copied_act")]
        prod_ready = sem("prod_ready")
        prod_copied = [sem("prod_copied_dve"), sem("prod_copied_act")]
        h1_summed = sem("h1_summed")
        h1_ready = sem("h1_ready")
        h2_summed = sem("h2_summed")
        h2_ready = sem("h2_ready")
        y_summed = sem("y_summed")
        y_ready = sem("y_ready")
        out_stored = sem("out_stored")

        block = ctx.enter_context(nc.Block())

        def group(j):
            return range(TRG * j, min(TRG * j + TRG, F))

        @block.sync
        def _(sp):
            for t, n in enumerate(TILES):
                sp.dma_start(ids_sb[0:n, t, :], ids[starts[t]:starts[t] + n, :]).then_inc(ids_loaded, 16)
            sp.dma_start(bottom_sb[:, :, :], bottom.rearrange("(c p) d -> p c d", p=128)).then_inc(bottom_loaded, 16)
            sp.dma_start(w1p_sb[:, :, :], w1p).then_inc(w1p_loaded, 16)
            sp.wait_ge(y_ready, len(TILES))
            sp.dma_start(out.rearrange("b o -> o b"), y_sb[:, :]).then_inc(out_stored, 16)
            sp.wait_ge(out_stored, 16)

        @block.gpsimd
        def _(pool):
            nc.gpsimd.memset(ident[:, :], 0.0).then_inc(ident_zeroed, 1)
            pool.wait_ge(ident_zeroed, 1)
            nc.gpsimd.affine_select(out=ident[:, :], in_=ident[:, :], compare_op=ALU.not_equal, fill=1.0,
                                    base=0, pattern=[[-1, 128]], channel_multiplier=1).then_inc(ident_made, 1)
            pool.wait_ge(ids_loaded, 16 * len(TILES))
            for t, n in enumerate(TILES):
                for j in range(TRS):
                    if t >= 2:
                        pool.wait_ge(turned_ready, TRS * (t - 2) + j + 1)
                    for f in group(j):
                        nc.gpsimd.indirect_dma_start(
                            out=gathered_sb[0:n, t % 2, f, :], out_offset=None, in_=tables[f],
                            in_offset=bass.IndirectOffsetOnAxis(ap=ids_sb[0:n, t, f:f + 1], axis=0),
                        ).then_inc(gathered[t % 2][j], 16)

        def copy_turned(copy, t, j):
            fs, n = group(j), TILES[t]
            return copy(turned[:, 0:n, fs[0]:fs[-1] + 1].rearrange("p b f -> p f b"),
                        turn_ps[:, (TRS * t + j) % 2, 0:len(fs), 0:n])

        def copy_blocks(copy, t, k, quads):
            m = first_batch[t] + k
            for q in quads:
                for s in range(QUADS):
                    cs = len(range(s, F, QUADS))
                    src = prod_ps[FP * q:FP * (q + 1), m % 2, :, F * q + s:F * (q + 1):QUADS]
                    dst = pairs[FP * s:FP * (s + 1), 0:cs, BATCH * k + q:BATCH * (k + 1):QUADS]
                    last = copy(dst.rearrange("p c b -> p b c"), src)
            return last

        def evacuate(eng, copy, side):
            def turns(t):
                for j in range(TRS):
                    n = TRS * t + j
                    if n % 2 == side:
                        eng.wait_ge(turned_ready, n + 1)
                        copy_turned(copy, t, j).then_inc(turn_copied[side], 1)

            def blocks(t):
                for k in range(batches[t]):
                    eng.wait_ge(prod_ready, first_batch[t] + k + 1)
                    copy_blocks(copy, t, k, (2 * side, 2 * side + 1)).then_inc(prod_copied[side], 1)
            return turns, blocks

        @block.vector
        def _(dve):
            nc.vector.memset(turned[:, :, F:FP], 0.0).then_inc(pads_set, 1)
            nc.vector.memset(pairs[FP * (QUADS - 1):128, CHUNKS - 1, :], 1.0).then_inc(pads_set, 1)
            dve.wait_ge(bottom_turned, 1)
            nc.vector.tensor_copy(bottom_t[:, :], h1_ps[:, :]).then_inc(bottom_copied, 1)
            turns, blocks = evacuate(dve, nc.vector.tensor_copy, 0)
            for t, n in enumerate(TILES):
                turns(t)
                if t == 0:
                    dve.wait_ge(w1b_loaded, 16)
                    nc.vector.tensor_tensor(w1s[:, :], w1b_sb[:, 0, :], w1b_sb[:, 1, :], ALU.add).then_inc(w1s_made, 1)
                blocks(t)
                dve.wait_ge(h1_summed, t + 1)
                nc.vector.tensor_scalar(h1[:, :, 0:n], h1_ps[:, :].rearrange("p (a b) -> p a b", a=NT1)[:, :, 0:n],
                                        0.0, None, ALU.max).then_inc(h1_ready, 1)
                dve.wait_ge(y_summed, t + 1)
                nc.vector.tensor_copy(y_sb[0:1, starts[t]:starts[t] + n], h2_ps[0:1, 256:256 + n]).then_inc(y_ready, 1)

        @block.scalar
        def _(act):
            act.dma_start(w1b_sb[:, :, :], w1b).then_inc(w1b_loaded, 16)
            act.dma_start(w2_sb[:, :, :], w2.rearrange("(k p) n -> p k n", p=128)).then_inc(w2_loaded, 16)
            act.dma_start(b2_sb[:, :], b2.rearrange("(m p) -> p m", p=128), allow_slow_non_contiguous=True).then_inc(small_loaded, 16)
            act.dma_start(w3_sb[:, :], w3.rearrange("(m p) o -> p (m o)", p=128), allow_slow_non_contiguous=True).then_inc(small_loaded, 16)
            act.wait_ge(small_loaded, 32)

            def copy(dst, src):
                return nc.scalar.activation(dst, src, ACT.Copy)

            turns, blocks = evacuate(act, copy, 1)
            for t, n in enumerate(TILES):
                turns(t)
                blocks(t)
                act.wait_ge(h2_summed, t + 1)
                for m in range(NT2):
                    nc.scalar.activation(h2[:, m, 0:n], h2_ps[:, 128 * m:128 * m + n], ACT.Relu,
                                         bias=b2_sb[:, m:m + 1]).then_inc(h2_ready, 1)

        @block.tensor
        def _(pe):
            pe.wait_ge(ident_made, 1)
            pe.wait_ge(bottom_loaded, 16)
            for c in range(B // 128):
                last = nc.tensor.transpose(h1_ps[:, 128 * c:128 * (c + 1)], bottom_sb[:, c, :], ident[:, :])
            last.then_inc(bottom_turned, 1)

            for t, n in enumerate(TILES):
                for j in range(TRS):
                    m = TRS * t + j
                    pe.wait_ge(gathered[t % 2][j], 16 * len(group(j)) * (t // 2 + 1))
                    if m >= 2:
                        pe.wait_ge(turn_copied[m % 2], m // 2)
                    for i, f in enumerate(group(j)):
                        last = nc.tensor.transpose(turn_ps[:, m % 2, i, 0:n], gathered_sb[0:n, t % 2, f, :],
                                                   ident[0:n, 0:n])
                    last.then_inc(turned_ready, 1)
                done = TRS * (t + 1)
                pe.wait_ge(turn_copied[0], (done + 1) // 2)
                pe.wait_ge(turn_copied[1], done // 2)
                if t == 0:
                    pe.wait_ge(pads_set, 2)
                for k in range(batches[t]):
                    m = first_batch[t] + k
                    if m >= 2:
                        pe.wait_ge(prod_copied[0], m - 1)
                        pe.wait_ge(prod_copied[1], m - 1)
                    for i in range(SPAN):
                        b = BATCH * k + QUADS * i
                        last = nc.tensor.matmul(prod_ps[:, m % 2, i, 0:QUADS * F], turned[:, b:b + QUADS, :],
                                                turned[:, b:b + QUADS, 0:F], start=True, stop=True)
                    last.then_inc(prod_ready, 1)
                if t == 0:
                    pe.wait_ge(bottom_copied, 1)
                    pe.wait_ge(w1s_made, 1)
                    pe.wait_ge(w1p_loaded, 16)
                else:
                    pe.wait_ge(h1_ready, t)
                pe.wait_ge(prod_copied[0], first_batch[t] + batches[t])
                pe.wait_ge(prod_copied[1], first_batch[t] + batches[t])
                for a in range(NT1):
                    acc = h1_ps[:, 128 * a:128 * a + n]
                    nc.tensor.matmul(acc, w1s[:, 128 * a:128 * (a + 1)], bottom_t[:, starts[t]:starts[t] + n],
                                     start=True, stop=False)
                    for c in range(CHUNKS):
                        last = nc.tensor.matmul(acc, w1p_sb[:, c, 128 * a:128 * (a + 1)], pairs[:, c, 0:n],
                                                start=False, stop=(c == CHUNKS - 1))
                last.then_inc(h1_summed, 1)
                if t == 0:
                    pe.wait_ge(w2_loaded, 16)
                else:
                    pe.wait_ge(y_ready, t)
                pe.wait_ge(h1_ready, t + 1)
                for m in range(NT2):
                    for a in range(NT1):
                        last = nc.tensor.matmul(h2_ps[:, 128 * m:128 * m + n], w2_sb[:, a, 128 * m:128 * (m + 1)],
                                                h1[:, a, 0:n], start=(a == 0), stop=(a == NT1 - 1))
                last.then_inc(h2_summed, 1)
                if t == 0:
                    pe.wait_ge(small_loaded, 32)
                pe.wait_ge(h2_ready, NT2 * (t + 1))
                for m in range(NT2):
                    last = nc.tensor.matmul(h2_ps[0:1, 256:256 + n], w3_sb[:, m:m + 1], h2[:, m, 0:n],
                                            start=(m == 0), stop=(m == NT2 - 1))
                last.then_inc(y_summed, 1)


def kernel(**inputs):
    import numpy as np
    import concourse.bacc as bacc
    from concourse.bass_utils import run_bass_kernel_spmd

    nc = bacc.Bacc("TRN2", target_bir_lowering=False, num_devices=1)
    arrays = {}

    def dram(name, a):
        arrays[name] = np.ascontiguousarray(a)
        return nc.dram_tensor(name, arrays[name].shape, mybir.dt.from_np(arrays[name].dtype), kind="ExternalInput").ap()

    w1 = np.asarray(inputs["W_top1"])
    w1p = np.zeros((QUADS, FP, CHUNKS, N1), w1.dtype)
    for f in range(F):
        for g in range(f):
            w1p[g % QUADS, f, g // QUADS] = w1[D + f * (f - 1) // 2 + g]
    w1p[QUADS - 1, 0, CHUNKS - 1] = np.asarray(inputs["b_top1"])
    w1b = np.stack([w1[:D], w1[D + PAIRS:]], axis=1)

    args = [
        dram("bottom_dram", inputs["r_bottom_mlp_out"]),
        dram("ids_dram", inputs["ids"]),
        [dram(f"tbl_{f}_dram", inputs[f"tbl_{f}"]) for f in range(F)],
        dram("w1p_dram", w1p.reshape(128, CHUNKS, N1)),
        dram("w1b_dram", w1b),
        dram("w2_dram", inputs["W_top2"]),
        dram("b2_dram", inputs["b_top2"]),
        dram("w3_dram", inputs["W_top3"]),
        nc.dram_tensor("y_dram", (B, 1), mybir.dt.float32, kind="ExternalOutput").ap(),
    ]
    build(nc, *args)
    r = run_bass_kernel_spmd(nc, [arrays], core_ids=[0])
    return r.results[0]["y_dram"]
```

```python
from contextlib import ExitStack

import concourse.bass as bass
from concourse import mybir

F = 27
D = 128
B = 512
FP = 32
QUADS = 128 // FP
CHUNKS = -(-F // QUADS)
PAIRS = F * (F - 1) // 2
G = F - 1
N1, N2 = 512, 256
NT1, NT2 = N1 // 128, N2 // 128
TILES = [128, 128, 128, 128]
VOCAB = [1250, 12500, 1000, 1250, 125000, 1250, 1000, 1250, 12500, 1250, 1250, 1000, 1000, 1250,
         12500, 12500, 1000, 12500, 12500, 12500, 12500, 1000, 1000, 1250, 1250, 1000, 1250]
HOT_CHUNKS = 8
HOT_TABLES = [f for f in range(F) if VOCAB[f] <= 128 * HOT_CHUNKS][:7]
COLD_TABLES = [f for f in range(F) if f not in HOT_TABLES]
HOT, COLD = len(HOT_TABLES), len(COLD_TABLES)
FEATURES = COLD_TABLES + HOT_TABLES
RAWS = 4
SPAN = 8
BATCH = SPAN * QUADS
TRG = 4
TRS = -(-COLD // TRG)
MAXT = max(TILES)
START = [("hot", 0)]
for _i in range(1, HOT):
    START.append(("hot", _i))
    if _i - 1 < TRS:
        START.append(("turn", _i - 1))
START += [("turn", _j) for _j in range(HOT - 1, TRS)]


def hot_fill(i):
    return START.index(("hot", i))


def turn_fill(t, j):
    return START.index(("turn", j)) if t == 0 else len(START) + TRS * (t - 1) + j


def copier(u):
    return 1 if u < len(START) else u % 2


def build(nc, bottom, ids, hot_ids, hot_rows, hot_tables, cold_tables, w1p, w1b, w2, b2, w3, out):
    fp32, fp32r, i32 = mybir.dt.float32, mybir.dt.float32r, mybir.dt.int32
    ALU = mybir.AluOpType
    ACT = mybir.ActivationFunctionType
    starts = [sum(TILES[:t]) for t in range(len(TILES))]
    batches = [n // BATCH for n in TILES]
    first_batch = [sum(batches[:t]) for t in range(len(TILES))]

    with ExitStack() as ctx:
        def sb(name, shape, dt=fp32):
            return ctx.enter_context(nc.sbuf_tensor(name, shape, dt))

        def ps(name, shape):
            return ctx.enter_context(nc.psum_tensor(name, shape, fp32))

        def sem(name):
            return ctx.enter_context(nc.semaphore(name))

        ids_sb = sb("ids_sb", [128, len(TILES), COLD], i32)
        hot_ids_sb = sb("hot_ids_sb", [128, HOT, B], i32)
        hot_rows_sb = sb("hot_rows_sb", [128, HOT_CHUNKS])
        raw = sb("raw", [128, RAWS, HOT_CHUNKS, D])
        upper = sb("upper", [128, 2, HOT_CHUNKS, D], fp32r)
        lower = sb("lower", [128, 2, HOT_CHUNKS, D], fp32r)
        onehot = sb("onehot", [128, HOT_CHUNKS, B], fp32r)
        gathered_sb = sb("gathered_sb", [128, 2, COLD, D])
        turned = sb("turned", [D, B, FP])
        pairs = sb("pairs", [128, CHUNKS, MAXT])
        bottom_sb = sb("bottom_sb", [128, B // 128, D])
        bottom_t = sb("bottom_t", [D, B])
        ident = sb("ident", [128, 128])
        w1p_sb = sb("w1p_sb", [128, CHUNKS, N1])
        w1b_sb = sb("w1b_sb", [D, 2, N1])
        w1s = sb("w1s", [D, N1])
        w2_sb = sb("w2_sb", [128, NT1, N2])
        b2_sb = sb("b2_sb", [128, NT2])
        w3_sb = sb("w3_sb", [128, NT2])
        h1 = sb("h1", [128, NT1, MAXT])
        h2 = sb("h2", [128, NT2, MAXT])
        y_sb = sb("y_sb", [1, B])

        feat_ps = ps("feat_ps", [128, 2, TRG, 128])
        prod_ps = ps("prod_ps", [128, 2, SPAN, 128])
        h1_ps = ps("h1_ps", [128, 512])
        h2_ps = ps("h2_ps", [128, 512])

        ids_loaded = sem("ids_loaded")
        hot_ids_loaded = [sem(f"hot_ids_loaded_{i}") for i in range(HOT)]
        hot_rows_loaded = sem("hot_rows_loaded")
        raw_loaded = [sem(f"raw_loaded_{r}") for r in range(RAWS)]
        upper_made = sem("upper_made")
        lower_made = sem("lower_made")
        onehot_made = sem("onehot_made")
        onehot_used = sem("onehot_used")
        bottom_loaded = sem("bottom_loaded")
        w1p_loaded = sem("w1p_loaded")
        w1b_loaded = sem("w1b_loaded")
        w2_loaded = sem("w2_loaded")
        small_loaded = sem("small_loaded")
        gathered = [[sem(f"gathered_{p}_{j}") for j in range(TRS)] for p in range(2)]
        ident_zeroed = sem("ident_zeroed")
        ident_made = sem("ident_made")
        pads_set = sem("pads_set")
        bottom_turned = sem("bottom_turned")
        bottom_copied = sem("bottom_copied")
        w1s_made = sem("w1s_made")
        feat_ready = sem("feat_ready")
        feat_copied = [sem("feat_copied_0"), sem("feat_copied_1")]
        prod_ready = sem("prod_ready")
        prod_copied = [sem("prod_copied_dve"), sem("prod_copied_act")]
        h1_summed = sem("h1_summed")
        h1_ready = sem("h1_ready")
        h2_summed = sem("h2_summed")
        h2_ready = sem("h2_ready")
        y_summed = sem("y_summed")
        y_ready = sem("y_ready")
        out_stored = sem("out_stored")

        block = ctx.enter_context(nc.Block())

        def group(j):
            return range(TRG * j, min(TRG * j + TRG, COLD))

        @block.sync
        def _(sp):
            sp.dma_start(ids_sb[:, :, :], ids.rearrange("(t p) f -> p t f", p=128)).then_inc(ids_loaded, 16)
            for i in range(HOT):
                sp.dma_start(hot_ids_sb[:, i, :], hot_ids[i].partition_broadcast(128)).then_inc(hot_ids_loaded[i], 16)
                if i >= RAWS:
                    sp.wait_ge(lower_made, i - RAWS + 1)
                sp.dma_start(raw[:, i % RAWS, :, :], hot_tables[i]).then_inc(raw_loaded[i % RAWS], 16)
            sp.dma_start(w1p_sb[:, :, :], w1p).then_inc(w1p_loaded, 16)
            sp.wait_ge(y_ready, len(TILES))
            sp.dma_start(out.rearrange("b o -> o b"), y_sb[:, :]).then_inc(out_stored, 16)
            sp.wait_ge(out_stored, 16)

        @block.gpsimd
        def _(pool):
            nc.gpsimd.memset(ident[:, :], 0.0).then_inc(ident_zeroed, 1)
            pool.wait_ge(ident_zeroed, 1)
            nc.gpsimd.affine_select(out=ident[:, :], in_=ident[:, :], compare_op=ALU.not_equal, fill=1.0,
                                    base=0, pattern=[[-1, 128]], channel_multiplier=1).then_inc(ident_made, 1)
            pool.wait_ge(ids_loaded, 16)
            for t, n in enumerate(TILES):
                for j in range(TRS):
                    if t >= 2:
                        pool.wait_ge(feat_ready, turn_fill(t - 2, j) + 1)
                    for f in group(j):
                        nc.gpsimd.indirect_dma_start(
                            out=gathered_sb[0:n, t % 2, f, :], out_offset=None, in_=cold_tables[f],
                            in_offset=bass.IndirectOffsetOnAxis(ap=ids_sb[0:n, t, f:f + 1], axis=0),
                        ).then_inc(gathered[t % 2][j], 16)

        def copy_turned(eng, copy, side, t, j):
            u, fs, n = turn_fill(t, j), group(j), TILES[t]
            if copier(u) == side:
                eng.wait_ge(feat_ready, u + 1)
                copy(turned[:, starts[t]:starts[t] + n, fs[0]:fs[-1] + 1].rearrange("p b f -> p f b"),
                     feat_ps[:, u % 2, 0:len(fs), 0:n]).then_inc(feat_copied[u % 2], 1)

        def copy_blocks(eng, copy, side, t, k):
            m = first_batch[t] + k
            eng.wait_ge(prod_ready, m + 1)
            for q in (2 * side, 2 * side + 1):
                for s in range(QUADS):
                    cs = len(range(s, G, QUADS))
                    src = prod_ps[FP * q:FP * (q + 1), m % 2, :, G * q + s:G * (q + 1):QUADS]
                    dst = pairs[FP * s:FP * (s + 1), 0:cs, BATCH * k + q:BATCH * (k + 1):QUADS]
                    last = copy(dst.rearrange("p c b -> p b c"), src)
            last.then_inc(prod_copied[side], 1)

        def turns_after(t, k):
            if t + 1 == len(TILES) or k == 0:
                return range(0)
            return range(k - 1, k if k < batches[t] - 1 else TRS)

        @block.vector
        def _(dve):
            def make_lower(i):
                dve.wait_ge(upper_made, i + 1)
                nc.vector.tensor_tensor(lower[:, i % 2, :, :], raw[:, i % RAWS, :, :],
                                        upper[:, i % 2, :, :].bitcast(fp32), ALU.subtract).then_inc(lower_made, 1)

            def make_onehot(i):
                dve.wait_ge(hot_ids_loaded[i], 16)
                for c in range(HOT_CHUNKS):
                    if i >= 1:
                        if c < HOT_CHUNKS - 1:
                            dve.wait_ge(onehot_used, (HOT_CHUNKS - 1) * (i - 1) + c + 1)
                        else:
                            dve.wait_ge(feat_ready, hot_fill(i - 1) + 1)
                    nc.vector.tensor_scalar(onehot[:, c, :], hot_ids_sb[:, i, :], hot_rows_sb[:, c:c + 1], None,
                                            ALU.is_equal).then_inc(onehot_made, 1)

            nc.vector.memset(turned[:, :, F:FP], 0.0).then_inc(pads_set, 1)
            nc.vector.memset(pairs[FP * (G % QUADS):128, CHUNKS - 1, :], 1.0).then_inc(pads_set, 1)
            dve.wait_ge(hot_rows_loaded, 16)
            make_onehot(0)
            for i in range(HOT):
                make_lower(i)
                if i >= 1:
                    make_onehot(i)
            dve.wait_ge(w1b_loaded, 16)
            nc.vector.tensor_tensor(w1s[:, :], w1b_sb[:, 0, :], w1b_sb[:, 1, :], ALU.add).then_inc(w1s_made, 1)

            def copy_y(t):
                dve.wait_ge(y_summed, t + 1)
                nc.vector.tensor_copy(y_sb[0:1, starts[t]:starts[t] + TILES[t]],
                                      h2_ps[0:1, 256:256 + TILES[t]]).then_inc(y_ready, 1)

            for t, n in enumerate(TILES):
                for k in range(batches[t]):
                    copy_blocks(dve, nc.vector.tensor_copy, 0, t, k)
                    for j in turns_after(t, k):
                        copy_turned(dve, nc.vector.tensor_copy, 0, t + 1, j)
                if t >= 1:
                    copy_y(t - 1)
                dve.wait_ge(h1_summed, t + 1)
                nc.vector.tensor_scalar(h1[:, :, 0:n], h1_ps[:, :].rearrange("p (a b) -> p a b", a=NT1)[:, :, 0:n],
                                        0.0, None, ALU.max).then_inc(h1_ready, 1)
            copy_y(len(TILES) - 1)

        @block.scalar
        def _(act):
            act.dma_start(hot_rows_sb[:, :], hot_rows).then_inc(hot_rows_loaded, 16)
            act.dma_start(bottom_sb[:, :, :], bottom.rearrange("(c p) d -> p c d", p=128)).then_inc(bottom_loaded, 16)
            act.dma_start(b2_sb[:, :], b2.rearrange("(m p) -> p m", p=128), allow_slow_non_contiguous=True).then_inc(small_loaded, 16)
            act.dma_start(w3_sb[:, :], w3.rearrange("(m p) o -> p (m o)", p=128), allow_slow_non_contiguous=True).then_inc(small_loaded, 16)

            def copy(dst, src):
                return nc.scalar.activation(dst, src, ACT.Copy)

            def make_upper(i):
                act.wait_ge(raw_loaded[i % RAWS], 16 * (i // RAWS + 1))
                if i >= 2:
                    act.wait_ge(feat_ready, hot_fill(i - 2) + 1)
                copy(upper[:, i % 2, :, :], raw[:, i % RAWS, :, :]).then_inc(upper_made, 1)

            make_upper(0)
            act.wait_ge(bottom_turned, 1)
            copy(bottom_t[:, :], h1_ps[:, :]).then_inc(bottom_copied, 1)
            make_upper(1)
            act.dma_start(w1b_sb[:, :, :], w1b).then_inc(w1b_loaded, 16)
            act.dma_start(w2_sb[:, :, :], w2.rearrange("(k p) n -> p k n", p=128)).then_inc(w2_loaded, 16)
            for u, (kind, i) in enumerate(START):
                act.wait_ge(feat_ready, u + 1)
                if kind == "hot":
                    copy(turned[:, :, COLD + i], feat_ps[:, u % 2, :, :]).then_inc(feat_copied[u % 2], 1)
                    if i + 2 < HOT:
                        make_upper(i + 2)
                else:
                    fs, n = group(i), TILES[0]
                    copy(turned[:, 0:n, fs[0]:fs[-1] + 1].rearrange("p b f -> p f b"),
                         feat_ps[:, u % 2, 0:len(fs), 0:n]).then_inc(feat_copied[u % 2], 1)

            def layer_2(t):
                act.wait_ge(h2_summed, t + 1)
                for m in range(NT2):
                    nc.scalar.activation(h2[:, m, 0:TILES[t]], h2_ps[:, 128 * m:128 * m + TILES[t]], ACT.Relu,
                                         bias=b2_sb[:, m:m + 1]).then_inc(h2_ready, 1)

            act.wait_ge(small_loaded, 32)
            for t in range(len(TILES)):
                for k in range(batches[t]):
                    copy_blocks(act, copy, 1, t, k)
                    if t >= 1 and k == 1:
                        layer_2(t - 1)
                    for j in turns_after(t, k):
                        copy_turned(act, copy, 1, t + 1, j)
            layer_2(len(TILES) - 1)

        @block.tensor
        def _(pe):
            def wait_bank(u):
                if u >= 2:
                    pe.wait_ge(feat_copied[u % 2], u // 2)

            def turn(t, j):
                u, n = turn_fill(t, j), TILES[t]
                pe.wait_ge(gathered[t % 2][j], 16 * len(group(j)) * (t // 2 + 1))
                wait_bank(u)
                for i, f in enumerate(group(j)):
                    last = nc.tensor.transpose(feat_ps[:, u % 2, i, 0:n], gathered_sb[0:n, t % 2, f, :],
                                               ident[0:n, 0:n])
                last.then_inc(feat_ready, 1)

            def pick(i):
                u = hot_fill(i)
                pe.wait_ge(upper_made, i + 1)
                pe.wait_ge(lower_made, i + 1)
                wait_bank(u)
                acc = feat_ps[:, u % 2, :, :]
                for c in range(HOT_CHUNKS):
                    pe.wait_ge(onehot_made, HOT_CHUNKS * i + c + 1)
                    nc.tensor.matmul(acc, upper[:, i % 2, c, :], onehot[:, c, :], start=(c == 0), stop=False)
                    last = nc.tensor.matmul(acc, lower[:, i % 2, c, :], onehot[:, c, :], start=False,
                                            stop=(c == HOT_CHUNKS - 1))
                    last.then_inc(onehot_used if c < HOT_CHUNKS - 1 else feat_ready, 1)

            def products(t, k):
                m = first_batch[t] + k
                if m >= 2:
                    pe.wait_ge(prod_copied[0], m - 1)
                    pe.wait_ge(prod_copied[1], m - 1)
                for i in range(SPAN):
                    b = starts[t] + BATCH * k + QUADS * i
                    last = nc.tensor.matmul(prod_ps[:, m % 2, i, 0:QUADS * G], turned[:, b:b + QUADS, :],
                                            turned[:, b:b + QUADS, 0:G], start=True, stop=True)
                last.then_inc(prod_ready, 1)

            def layer_1(t):
                n = TILES[t]
                if t >= 1:
                    pe.wait_ge(h1_ready, t)
                pe.wait_ge(prod_copied[0], first_batch[t] + batches[t])
                pe.wait_ge(prod_copied[1], first_batch[t] + batches[t])
                for a in range(NT1):
                    acc = h1_ps[:, 128 * a:128 * a + n]
                    nc.tensor.matmul(acc, w1s[:, 128 * a:128 * (a + 1)], bottom_t[:, starts[t]:starts[t] + n],
                                     start=True, stop=False)
                    for c in range(CHUNKS):
                        last = nc.tensor.matmul(acc, w1p_sb[:, c, 128 * a:128 * (a + 1)], pairs[:, c, 0:n],
                                                start=False, stop=(c == CHUNKS - 1))
                last.then_inc(h1_summed, 1)

            def layer_2(t):
                n = TILES[t]
                if t >= 1:
                    pe.wait_ge(y_ready, t)
                pe.wait_ge(h1_ready, t + 1)
                for m in range(NT2):
                    for a in range(NT1):
                        last = nc.tensor.matmul(h2_ps[:, 128 * m:128 * m + n], w2_sb[:, a, 128 * m:128 * (m + 1)],
                                                h1[:, a, 0:n], start=(a == 0), stop=(a == NT1 - 1))
                last.then_inc(h2_summed, 1)

            def layer_3(t):
                n = TILES[t]
                pe.wait_ge(h2_ready, NT2 * (t + 1))
                for m in range(NT2):
                    last = nc.tensor.matmul(h2_ps[0:1, 256:256 + n], w3_sb[:, m:m + 1], h2[:, m, 0:n],
                                            start=(m == 0), stop=(m == NT2 - 1))
                last.then_inc(y_summed, 1)

            pe.wait_ge(ident_made, 1)
            pe.wait_ge(bottom_loaded, 16)
            for c in range(B // 128):
                last = nc.tensor.transpose(h1_ps[:, 128 * c:128 * (c + 1)], bottom_sb[:, c, :], ident[:, :])
            last.then_inc(bottom_turned, 1)
            for kind, i in START:
                if kind == "hot":
                    pick(i)
                else:
                    turn(0, i)
            pe.wait_ge(pads_set, 2)
            pe.wait_ge(w1p_loaded, 16)
            pe.wait_ge(w2_loaded, 16)
            pe.wait_ge(small_loaded, 32)
            pe.wait_ge(w1s_made, 1)
            pe.wait_ge(bottom_copied, 1)
            for t in range(len(TILES)):
                last_fill = turn_fill(t, TRS - 1) if t else len(START) - 1
                for u in (last_fill - 1, last_fill):
                    pe.wait_ge(feat_copied[u % 2], u // 2 + 1)
                for k in range(batches[t]):
                    products(t, k)
                    if t >= 1 and k == 1:
                        layer_2(t - 1)
                    for j in turns_after(t, k):
                        turn(t + 1, j)
                if t >= 1:
                    layer_3(t - 1)
                layer_1(t)
            layer_2(len(TILES) - 1)
            layer_3(len(TILES) - 1)


def kernel(**inputs):
    import numpy as np
    import concourse.bacc as bacc
    from concourse.bass_utils import run_bass_kernel_spmd

    nc = bacc.Bacc("TRN2", target_bir_lowering=False, num_devices=1)
    arrays = {}

    def dram(name, a):
        arrays[name] = np.ascontiguousarray(a)
        return nc.dram_tensor(name, arrays[name].shape, mybir.dt.from_np(arrays[name].dtype), kind="ExternalInput").ap()

    w1 = np.asarray(inputs["W_top1"])
    w1p = np.zeros((QUADS, FP, CHUNKS, N1), w1.dtype)
    for f in range(F):
        for g in range(f):
            hi, lo = max(FEATURES[f], FEATURES[g]), min(FEATURES[f], FEATURES[g])
            w1p[g % QUADS, f, g // QUADS] = w1[D + hi * (hi - 1) // 2 + lo]
    w1p[QUADS - 1, 0, CHUNKS - 1] = np.asarray(inputs["b_top1"])
    w1b = np.stack([w1[:D], w1[D + PAIRS:]], axis=1)

    rows = 128 * HOT_CHUNKS
    hot = np.zeros((HOT, rows, D), np.float32)
    for i, f in enumerate(HOT_TABLES):
        hot[i, :VOCAB[f]] = np.asarray(inputs[f"tbl_{f}"])
    ids = np.asarray(inputs["ids"])

    args = [
        dram("bottom_dram", inputs["r_bottom_mlp_out"]),
        dram("ids_dram", ids[:, COLD_TABLES]),
        dram("hot_ids_dram", ids[:, HOT_TABLES].T),
        dram("hot_rows_dram", np.arange(rows, dtype=np.float32).reshape(128, HOT_CHUNKS)),
        dram("hot_tables_dram", hot.reshape(HOT, 128, HOT_CHUNKS, D)),
        [dram(f"tbl_{f}_dram", inputs[f"tbl_{f}"]) for f in COLD_TABLES],
        dram("w1p_dram", w1p.reshape(128, CHUNKS, N1)),
        dram("w1b_dram", w1b),
        dram("w2_dram", inputs["W_top2"]),
        dram("b2_dram", inputs["b_top2"]),
        dram("w3_dram", inputs["W_top3"]),
        nc.dram_tensor("y_dram", (B, 1), mybir.dt.float32, kind="ExternalOutput").ap(),
    ]
    build(nc, *args)
    r = run_bass_kernel_spmd(nc, [arrays], core_ids=[0])
    return r.results[0]["y_dram"]
```

```python
from contextlib import ExitStack

import concourse.bass as bass
from concourse import mybir

F = 27
D = 128
B = 512
FP = 32
QUADS = 128 // FP
CHUNKS = -(-F // QUADS)
PAIRS = F * (F - 1) // 2
G = F - 1
ROWS = (QUADS - 1) * FP + G
N1, N2 = 512, 256
NT1, NT2 = N1 // 128, N2 // 128
TILES = [128, 128, 128, 128]
VOCAB = [1250, 12500, 1000, 1250, 125000, 1250, 1000, 1250, 12500, 1250, 1250, 1000, 1000, 1250,
         12500, 12500, 1000, 12500, 12500, 12500, 12500, 1000, 1000, 1250, 1250, 1000, 1250]
HOT_CHUNKS = 8
HOT_TABLES = [f for f in range(F) if VOCAB[f] <= 128 * HOT_CHUNKS]
COLD_TABLES = [f for f in range(F) if f not in HOT_TABLES]
HOT, COLD = len(HOT_TABLES), len(COLD_TABLES)
FEATURES = COLD_TABLES + HOT_TABLES
RAWS = 4
PACKS = [[0, 5, 6], [1, 4], [2, 3]]
PACKED = [[(f, g) for c in cs for g in range(4 * c, min(4 * c + 4, F - 1)) for f in range(g + 1, F)] for cs in PACKS]
assert sorted(p for ps in PACKED for p in ps) == [(f, g) for f in range(F) for g in range(f)]
assert max(map(len, PACKED)) < 128
ONES_ROW = len(PACKED[0])
SPAN = 8
BATCH = SPAN * QUADS
TRG = 4
TRS = -(-COLD // TRG)
MAXT = max(TILES)
LAST = len(TILES) - 1
BOTTOM_AFTER = HOT - 1
WARM_UP = 12

TURNS = [[0, 1, 1, 1, 0, 1, 1], [1, 0, 1, 0, 1, 0, 2], [0, 1, 0, 1, 0, 1, 2], [0] * 7]
AHEAD_OF_PACK, AHEAD_OF_LAYER_1, IN_LAYER_1 = range(len(TURNS[0]) - 3, len(TURNS[0]))
assert all(sum(c) == TRS for c in TURNS[:-1]) and len(TURNS) == len(TILES)


def turns_before_pack(t):
    return sum(TURNS[t][:-2])


def turn_fill(t, j):
    return HOT + (TRS + 1) * (t - 1) + j + (j >= turns_before_pack(t - 1))


def pack_fill(t):
    return HOT + (TRS + 1) * t + turns_before_pack(t)


def copier(u):
    return u % 2


def build(nc, bottom, ids, hot_ids, hot_offsets, hot_tables, cold_tables, packing, w1p, w1b, w2, b2, w3, out):
    fp32, fp32r, i32 = mybir.dt.float32, mybir.dt.float32r, mybir.dt.int32
    ALU = mybir.AluOpType
    ACT = mybir.ActivationFunctionType
    starts = [sum(TILES[:t]) for t in range(len(TILES))]
    batches = [n // BATCH for n in TILES]
    first_batch = [sum(batches[:t]) for t in range(len(TILES))]

    with ExitStack() as ctx:
        def sb(name, shape, dt=fp32):
            return ctx.enter_context(nc.sbuf_tensor(name, shape, dt))

        def ps(name, shape):
            return ctx.enter_context(nc.psum_tensor(name, shape, fp32))

        def sem(name):
            return ctx.enter_context(nc.semaphore(name))

        ids_sb = sb("ids_sb", [128, len(TILES), COLD], i32)
        hot_ids_sb = sb("hot_ids_sb", [128, HOT, B], i32)
        hot_offsets_sb = sb("hot_offsets_sb", [128, 2])
        shifted = sb("shifted", [128, 2, 2, B])
        raw = sb("raw", [128, RAWS, HOT_CHUNKS, D])
        upper = sb("upper", [128, 2, HOT_CHUNKS, D], fp32r)
        lower = sb("lower", [128, 2, HOT_CHUNKS, D], fp32r)
        onehot = sb("onehot", [128, HOT_CHUNKS, B], fp32r)
        gathered_sb = sb("gathered_sb", [128, 2, COLD, D])
        turned = sb("turned", [D, B, FP])
        pairs = sb("pairs", [128, CHUNKS, MAXT])
        bottom_sb = sb("bottom_sb", [128, B // 128, D])
        bottom_t = sb("bottom_t", [D, B])
        ident = sb("ident", [128, 128])
        packing_sb = sb("packing_sb", [128, CHUNKS, 128])
        packed = sb("packed", [128, len(PACKS), MAXT])
        w1p_sb = sb("w1p_sb", [128, len(PACKS), N1])
        w1b_sb = sb("w1b_sb", [D, 2, N1])
        w1s = sb("w1s", [D, N1])
        w2_sb = sb("w2_sb", [128, NT1, N2])
        b2_sb = sb("b2_sb", [128, NT2])
        w3_sb = sb("w3_sb", [128, NT2])
        h1 = sb("h1", [128, NT1, MAXT])
        h2 = sb("h2", [128, NT2, MAXT])
        y_sb = sb("y_sb", [1, B])

        feat_ps = ps("feat_ps", [128, 2, TRG, 128])
        prod_ps = ps("prod_ps", [128, 2, SPAN, 128])
        h1_ps = ps("h1_ps", [128, 512])
        h2_ps = ps("h2_ps", [128, 512])

        ids_loaded = sem("ids_loaded")
        hot_ids_loaded = [sem(f"hot_ids_loaded_{i}") for i in range(HOT)]
        hot_offsets_loaded = sem("hot_offsets_loaded")
        shifted_made = sem("shifted_made")
        packing_loaded = sem("packing_loaded")
        raw_loaded = [sem(f"raw_loaded_{r}") for r in range(RAWS)]
        upper_made = sem("upper_made")
        lower_made = sem("lower_made")
        onehot_made = sem("onehot_made")
        onehot_used = sem("onehot_used")
        bottom_loaded = sem("bottom_loaded")
        w1p_loaded = sem("w1p_loaded")
        w1b_loaded = sem("w1b_loaded")
        w2_loaded = sem("w2_loaded")
        small_loaded = sem("small_loaded")
        gathered = [[sem(f"gathered_{p}_{j}") for j in range(TRS)] for p in range(2)]
        ident_zeroed = sem("ident_zeroed")
        ident_made = sem("ident_made")
        pads_set = sem("pads_set")
        table_warm = sem("table_warm")
        bottom_turned = sem("bottom_turned")
        bottom_copied = sem("bottom_copied")
        w1s_made = sem("w1s_made")
        feat_ready = sem("feat_ready")
        feat_copied = [sem("feat_copied_0"), sem("feat_copied_1")]
        turn0_ready = sem("turn0_ready")
        turn0_copied = sem("turn0_copied")
        prod_ready = sem("prod_ready")
        prod_copied = [sem("prod_copied_dve"), sem("prod_copied_act")]
        h1_summed = sem("h1_summed")
        h1_ready = sem("h1_ready")
        h2_summed = sem("h2_summed")
        h2_ready = sem("h2_ready")
        y_summed = sem("y_summed")
        y_ready = sem("y_ready")
        out_stored = sem("out_stored")

        block = ctx.enter_context(nc.Block())

        def h1_part(t, a):
            return prod_ps[:, 0, a - NT1 // 2, 0:TILES[t]] if t == LAST and a >= NT1 // 2 else \
                h1_ps[:, 128 * a:128 * a + TILES[t]]

        def h1_halves(t):
            return [range(NT1 // 2), range(NT1 // 2, NT1)] if t == LAST else [range(NT1)]

        def h2_part(t, m):
            return prod_ps[:, 1, 0, 0:TILES[t]] if t == LAST and m >= 1 else h2_ps[:, 128 * m:128 * m + TILES[t]]

        def group(j):
            return range(TRG * j, min(TRG * j + TRG, COLD))

        @block.sync
        def _(sp):
            sp.dma_start(ids_sb[:, :, :], ids.rearrange("(t p) f -> p t f", p=128)).then_inc(ids_loaded, 16)
            for i in range(HOT):
                sp.dma_start(hot_ids_sb[:, i, :], hot_ids[i].partition_broadcast(128)).then_inc(hot_ids_loaded[i], 16)
                if i >= RAWS:
                    sp.wait_ge(lower_made, i - RAWS + 1)
                sp.dma_start(raw[:, i % RAWS, :, :], hot_tables[i]).then_inc(raw_loaded[i % RAWS], 16)
            sp.dma_start(bottom_sb[:, :, :], bottom.rearrange("(c p) d -> p c d", p=128)).then_inc(bottom_loaded, 16)
            sp.dma_start(w1b_sb[:, :, :], w1b).then_inc(w1b_loaded, 16)
            sp.dma_start(packing_sb[:, :, :], packing).then_inc(packing_loaded, 16)
            sp.dma_start(w1p_sb[:, :, :], w1p).then_inc(w1p_loaded, 16)
            sp.dma_start(b2_sb[:, :], b2.rearrange("(m p) -> p m", p=128),
                         allow_slow_non_contiguous=True).then_inc(small_loaded, 16)
            sp.dma_start(w3_sb[:, :], w3.rearrange("(m p) o -> p (m o)", p=128),
                         allow_slow_non_contiguous=True).then_inc(small_loaded, 16)
            sp.dma_start(w2_sb[:, :, :], w2.rearrange("(k p) n -> p k n", p=128)).then_inc(w2_loaded, 16)
            sp.wait_ge(y_ready, len(TILES))
            sp.dma_start(out.rearrange("b o -> o b"), y_sb[:, :]).then_inc(out_stored, 16)
            sp.wait_ge(out_stored, 16)

        @block.gpsimd
        def _(pool):
            nc.gpsimd.memset(ident[:, :], 0.0).then_inc(ident_zeroed, 1)
            pool.wait_ge(ident_zeroed, 1)
            nc.gpsimd.affine_select(out=ident[:, :], in_=ident[:, :], compare_op=ALU.not_equal, fill=1.0,
                                    base=0, pattern=[[-1, 128]], channel_multiplier=1).then_inc(ident_made, 1)
            pool.wait_ge(ids_loaded, 16)
            for t, n in enumerate(TILES):
                for j in range(TRS):
                    if t >= 2:
                        if t == 2:
                            pool.wait_ge(turn0_ready, j + 1)
                        else:
                            pool.wait_ge(feat_ready, turn_fill(t - 2, j) + 1)
                    for f in group(j):
                        nc.gpsimd.indirect_dma_start(
                            out=gathered_sb[0:n, t % 2, f, :], out_offset=None, in_=cold_tables[f],
                            in_offset=bass.IndirectOffsetOnAxis(ap=ids_sb[0:n, t, f:f + 1], axis=0),
                        ).then_inc(gathered[t % 2][j], 16)

        def copy_turned(eng, copy, side, t, j):
            u, fs, n = turn_fill(t, j), group(j), TILES[t]
            if copier(u) == side:
                eng.wait_ge(feat_ready, u + 1)
                copy(turned[:, starts[t]:starts[t] + n, fs[0]:fs[-1] + 1].rearrange("p b f -> p f b"),
                     feat_ps[:, u % 2, 0:len(fs), 0:n]).then_inc(feat_copied[u % 2], 1)

        def copy_blocks(eng, copy, side, t, k):
            m = first_batch[t] + k
            eng.wait_ge(prod_ready, m + 1)
            for q in (2 * side, 2 * side + 1):
                for s in range(QUADS):
                    cs = len(range(s, G, QUADS))
                    src = prod_ps[FP * q:FP * q + G, m % 2, :, G * q + s:G * (q + 1):QUADS]
                    dst = pairs[FP * s:FP * s + G, 0:cs, BATCH * k + q:BATCH * (k + 1):QUADS]
                    last = copy(dst.rearrange("p c b -> p b c"), src)
            last.then_inc(prod_copied[side], 1)

        def first_turns(i):
            j = i - (HOT - 1 - TRS)
            return range(j, j + 1) if 0 <= j < TRS else range(0)

        def turns_at(t, k):
            first = sum(TURNS[t][:k])
            return range(first, first + TURNS[t][k])

        def copy_packed(eng, copy, side, t):
            u = pack_fill(t)
            if copier(u) == side:
                eng.wait_ge(feat_ready, u + 1)
                copy(packed[:, :, 0:TILES[t]],
                     feat_ps[:, u % 2, 0:len(PACKS), 0:TILES[t]]).then_inc(feat_copied[u % 2], 1)
            for k in (AHEAD_OF_LAYER_1, IN_LAYER_1):
                for j in turns_at(t, k):
                    copy_turned(eng, copy, side, t + 1, j)

        @block.vector
        def _(dve):
            def make_lower(i):
                dve.wait_ge(upper_made, i + 1)
                nc.vector.tensor_tensor(lower[:, i % 2, :, :], raw[:, i % RAWS, :, :],
                                        upper[:, i % 2, :, :].bitcast(fp32), ALU.subtract).then_inc(lower_made, 1)

            def make_onehot(i):
                dve.wait_ge(shifted_made, i)
                for c in range(0, HOT_CHUNKS, 2):
                    if c < HOT_CHUNKS - 2:
                        dve.wait_ge(onehot_used, (HOT_CHUNKS // 2 - 1) * (i - 1) + c // 2 + 1)
                    else:
                        dve.wait_ge(feat_ready, i)
                    nc.vector.tensor_scalar(onehot[:, c:c + 2, :], shifted[:, i % 2, :, :], float(c), None,
                                            ALU.is_equal).then_inc(onehot_made, 1)

            nc.vector.memset(pairs[:, 0:CHUNKS - 1, :], 0.0).then_inc(pads_set, 1)
            nc.vector.memset(pairs[0:FP * (G % QUADS), CHUNKS - 1, :], 0.0).then_inc(pads_set, 1)
            nc.vector.memset(pairs[FP * (G % QUADS):128, CHUNKS - 1, :], 1.0).then_inc(pads_set, 1)
            nc.vector.memset(turned[:, :, F:FP], 0.0).then_inc(pads_set, 1)
            dve.wait_ge(hot_offsets_loaded, 16)
            dve.wait_ge(hot_ids_loaded[0], 16)
            for c in range(HOT_CHUNKS):
                last = nc.vector.tensor_scalar(onehot[:, c, :], hot_ids_sb[:, 0, :], hot_offsets_sb[:, 0:1], float(c),
                                               ALU.add, ALU.is_equal)
                if c % 2 == 1:
                    last.then_inc(onehot_made, 1)
            make_lower(0)
            for i in range(1, HOT):
                make_lower(i)
                make_onehot(i)
            dve.wait_ge(w1b_loaded, 16)
            nc.vector.tensor_tensor(w1s[:, :], w1b_sb[:, 0, :], w1b_sb[:, 1, :], ALU.add).then_inc(w1s_made, 1)

            def copy_y(t):
                dve.wait_ge(y_summed, t + 1)
                nc.vector.tensor_copy(y_sb[0:1, starts[t]:starts[t] + TILES[t]],
                                      h2_ps[0:1, 256:256 + TILES[t]]).then_inc(y_ready, 1)

            for t, n in enumerate(TILES):
                for k in range(batches[t]):
                    for j in turns_at(t, k):
                        copy_turned(dve, nc.vector.tensor_copy, 0, t + 1, j)
                    copy_blocks(dve, nc.vector.tensor_copy, 0, t, k)
                for j in turns_at(t, AHEAD_OF_PACK):
                    copy_turned(dve, nc.vector.tensor_copy, 0, t + 1, j)
                copy_packed(dve, nc.vector.tensor_copy, 0, t)
                if t >= 1:
                    copy_y(t - 1)
                for i, parts in enumerate(h1_halves(t)):
                    dve.wait_ge(h1_summed, t + i + 1)
                    src = prod_ps[:, 0, 0:len(parts), 0:n] if i else \
                        h1_ps[:, :].rearrange("p (a b) -> p a b", a=NT1)[:, 0:len(parts), 0:n]
                    nc.vector.tensor_scalar(h1[:, parts[0]:parts[-1] + 1, 0:n], src,
                                            0.0, None, ALU.max).then_inc(h1_ready, 1)
            copy_y(len(TILES) - 1)

        @block.scalar
        def _(act):
            act.dma_start(hot_offsets_sb[:, :], hot_offsets).then_inc(hot_offsets_loaded, 16)

            def copy(dst, src):
                return nc.scalar.activation(dst, src, ACT.Copy)

            def make_upper(i):
                act.wait_ge(raw_loaded[i % RAWS], 16 * (i // RAWS + 1))
                if i >= 2:
                    act.wait_ge(feat_ready, i - 1)
                copy(upper[:, i % 2, :, :], raw[:, i % RAWS, :, :]).then_inc(upper_made, 1)

            def make_shifted(i):
                act.wait_ge(hot_ids_loaded[i], 16)
                if i >= 3:
                    act.wait_ge(onehot_made, HOT_CHUNKS // 2 * (i - 1))
                for e in range(2):
                    last = nc.scalar.activation(shifted[:, i % 2, e, :], hot_ids_sb[:, i, :], ACT.Identity,
                                                bias=hot_offsets_sb[:, e:e + 1])
                last.then_inc(shifted_made, 1)

            act.wait_ge(pads_set, 3)
            nc.scalar.activation(h2[96:128, 0, 0:1], pairs[96:128, CHUNKS - 1, 0:1], ACT.Identity).then_inc(table_warm, 1)
            act.wait_ge(hot_offsets_loaded, 16)
            make_upper(0)
            make_shifted(1)
            make_upper(1)
            for i in range(HOT):
                if i + 2 < HOT:
                    make_shifted(i + 2)
                    make_upper(i + 2)
                act.wait_ge(feat_ready, i + 1)
                copy(turned[:, :, COLD + i], feat_ps[:, i % 2, :, :]).then_inc(feat_copied[i % 2], 1)
                if i == BOTTOM_AFTER:
                    act.wait_ge(bottom_turned, 1)
                    copy(bottom_t[:, :], h1_ps[:, :]).then_inc(bottom_copied, 1)
                for j in first_turns(i):
                    fs, n = group(j), TILES[0]
                    act.wait_ge(turn0_ready, j + 1)
                    copy(turned[:, 0:n, fs[0]:fs[-1] + 1].rearrange("p b f -> p f b"),
                         h2_ps[:, :].rearrange("p (i b) -> p i b", i=TRG)[:, 0:len(fs), 0:n]).then_inc(turn0_copied, 1)

            def layer_2(t):
                for m in range(NT2):
                    act.wait_ge(h2_summed, NT2 * t + m + 1 if t == LAST else NT2 * (t + 1))
                    nc.scalar.activation(h2[:, m, 0:TILES[t]], h2_part(t, m), ACT.Relu,
                                         bias=b2_sb[:, m:m + 1]).then_inc(h2_ready, 1)

            act.wait_ge(small_loaded, 32)
            for t in range(len(TILES)):
                for k in range(batches[t]):
                    for j in turns_at(t, k):
                        copy_turned(act, copy, 1, t + 1, j)
                    copy_blocks(act, copy, 1, t, k)
                for j in turns_at(t, AHEAD_OF_PACK):
                    copy_turned(act, copy, 1, t + 1, j)
                if t >= 1:
                    layer_2(t - 1)
                copy_packed(act, copy, 1, t)
            layer_2(len(TILES) - 1)

        @block.tensor
        def _(pe):
            def wait_bank(u):
                if u >= 2:
                    pe.wait_ge(feat_copied[u % 2], u // 2)

            def turn(t, j):
                n = TILES[t]
                pe.wait_ge(gathered[t % 2][j], 16 * len(group(j)) * (t // 2 + 1))
                if t == 0:
                    bank = h2_ps[:, :].rearrange("p (i b) -> p i b", i=TRG)
                    if j >= 1:
                        pe.wait_ge(turn0_copied, j)
                else:
                    bank = feat_ps[:, turn_fill(t, j) % 2, :, :]
                    wait_bank(turn_fill(t, j))
                for i, f in enumerate(group(j)):
                    last = nc.tensor.transpose(bank[:, i, 0:n], gathered_sb[0:n, t % 2, f, :], ident[0:n, 0:n])
                last.then_inc(turn0_ready if t == 0 else feat_ready, 1)

            def pick(i):
                wait_bank(i)
                acc = feat_ps[:, i % 2, :, :]
                steps = [(h, c) for c in range(HOT_CHUNKS) for h in (upper, lower)] if i else \
                        [(h, c) for h in (upper, lower) for c in range(HOT_CHUNKS)]
                pe.wait_ge(upper_made, i + 1)
                if i >= 1:
                    pe.wait_ge(lower_made, i + 1)
                for n, (half, c) in enumerate(steps):
                    if half is upper and c % 2 == 0:
                        pe.wait_ge(onehot_made, HOT_CHUNKS // 2 * i + c // 2 + 1)
                    if i == 0 and half is lower and c == 0:
                        pe.wait_ge(lower_made, 1)
                    last = nc.tensor.matmul(acc, half[:, i % 2, c, :], onehot[:, c, :], start=(n == 0),
                                            stop=(n == len(steps) - 1))
                    if half is lower and c % 2 == 1:
                        last.then_inc(onehot_used if c < HOT_CHUNKS - 1 else feat_ready, 1)

            def products(t, k):
                m = first_batch[t] + k
                if m >= 2:
                    pe.wait_ge(prod_copied[0], m - 1)
                    pe.wait_ge(prod_copied[1], m - 1)
                for i in range(SPAN):
                    b = starts[t] + BATCH * k + QUADS * i
                    last = nc.tensor.matmul(prod_ps[0:ROWS, m % 2, i, 0:QUADS * G],
                                            turned[:, b:b + QUADS, :].rearrange("p b f -> p (b f)")[:, 1:1 + ROWS],
                                            turned[:, b:b + QUADS, 0:G], start=True, stop=True)
                last.then_inc(prod_ready, 1)

            def pack(t):
                u, n = pack_fill(t), TILES[t]
                wait_bank(u)
                if t == 0:
                    pe.wait_ge(packing_loaded, 16)
                pe.wait_ge(prod_copied[0], first_batch[t] + batches[t])
                pe.wait_ge(prod_copied[1], first_batch[t] + batches[t])
                for i, cs in enumerate(PACKS):
                    for c in cs:
                        last = nc.tensor.matmul(feat_ps[:, u % 2, i, 0:n], packing_sb[:, c, :], pairs[:, c, 0:n],
                                                start=(c == cs[0]), stop=(c == cs[-1]))
                last.then_inc(feat_ready, 1)

            def layer_1_bottom(t):
                n = TILES[t]
                if t == 0:
                    pe.wait_ge(bottom_copied, 1)
                    pe.wait_ge(w1s_made, 1)
                else:
                    pe.wait_ge(h1_ready, t)
                for a in range(NT1):
                    nc.tensor.matmul(h1_part(t, a), w1s[:, 128 * a:128 * (a + 1)],
                                     bottom_t[:, starts[t]:starts[t] + n],
                                     start=any(a == parts[0] for parts in h1_halves(t)), stop=False,
                                     skip_group_check=True)

            def layer_1(t):
                n, u = TILES[t], pack_fill(t)
                if t == 0:
                    pe.wait_ge(w1p_loaded, 16)
                pe.wait_ge(feat_copied[u % 2], u // 2 + 1)
                for parts in h1_halves(t):
                    for c in range(len(PACKS)):
                        if c == len(PACKS) - 1:
                            for j in turns_at(t, IN_LAYER_1):
                                turn(t + 1, j)
                        for a in parts:
                            last = nc.tensor.matmul(h1_part(t, a), w1p_sb[:, c, 128 * a:128 * (a + 1)],
                                                    packed[:, c, 0:n], start=False, stop=(c == len(PACKS) - 1),
                                                    skip_group_check=True)
                    last.then_inc(h1_summed, 1)

            def layer_2(t):
                n = TILES[t]
                if t >= 1:
                    pe.wait_ge(y_ready, t)
                else:
                    pe.wait_ge(w2_loaded, 16)
                    pe.wait_ge(small_loaded, 32)
                for i, parts in enumerate(h1_halves(t)):
                    pe.wait_ge(h1_ready, t + i + 1)
                    for m in range(NT2):
                        for a in parts:
                            last = nc.tensor.matmul(h2_part(t, m), w2_sb[:, a, 128 * m:128 * (m + 1)], h1[:, a, 0:n],
                                                    start=(a == 0), stop=(a == NT1 - 1))
                        if a == NT1 - 1:
                            last.then_inc(h2_summed, 1)

            def layer_3(t):
                n = TILES[t]
                for m in range(NT2):
                    pe.wait_ge(h2_ready, NT2 * t + m + 1 if t == LAST else NT2 * (t + 1))
                    last = nc.tensor.matmul(h2_ps[0:1, 256:256 + n], w3_sb[:, m:m + 1], h2[:, m, 0:n],
                                            start=(m == 0), stop=(m == NT2 - 1))
                last.then_inc(y_summed, 1)

            pe.wait_ge(ident_made, 1)
            for _ in range(WARM_UP):
                nc.tensor.matmul(h2_ps[:, 0:128], ident[:, :], ident[:, :], start=True, stop=True)
            for i in range(HOT):
                pick(i)
                if i == BOTTOM_AFTER:
                    pe.wait_ge(bottom_loaded, 16)
                    for c in range(B // 128):
                        last = nc.tensor.transpose(h1_ps[:, 128 * c:128 * (c + 1)], bottom_sb[:, c, :], ident[:, :])
                    last.then_inc(bottom_turned, 1)
                for j in first_turns(i):
                    turn(0, j)
            pe.wait_ge(pads_set, 4)
            for t in range(len(TILES)):
                for k in range(batches[t]):
                    for j in turns_at(t, k):
                        turn(t + 1, j)
                    if k == 0:
                        for u in ((turn_fill(t, TRS - 2), turn_fill(t, TRS - 1)) if t else (HOT - 2, HOT - 1)):
                            pe.wait_ge(feat_copied[u % 2], u // 2 + 1)
                        if t == 0:
                            pe.wait_ge(turn0_copied, TRS)
                    products(t, k)
                for j in turns_at(t, AHEAD_OF_PACK):
                    turn(t + 1, j)
                if t >= 1:
                    layer_2(t - 1)
                else:
                    layer_1_bottom(t)
                pack(t)
                for j in turns_at(t, AHEAD_OF_LAYER_1):
                    turn(t + 1, j)
                if t >= 1:
                    layer_1_bottom(t)
                    layer_3(t - 1)
                layer_1(t)
            layer_2(len(TILES) - 1)
            layer_3(len(TILES) - 1)


def kernel(**inputs):
    import numpy as np
    import concourse.bacc as bacc
    from concourse.bass_utils import run_bass_kernel_spmd

    nc = bacc.Bacc("TRN2", target_bir_lowering=False, num_devices=1)
    arrays = {}

    def dram(name, a):
        arrays[name] = np.ascontiguousarray(a)
        return nc.dram_tensor(name, arrays[name].shape, mybir.dt.from_np(arrays[name].dtype), kind="ExternalInput").ap()

    w1 = np.asarray(inputs["W_top1"])
    w1p = np.zeros((128, len(PACKS), N1), w1.dtype)
    packing = np.zeros((QUADS, FP, CHUNKS, 128), np.float32)
    for c, rows in enumerate(PACKED):
        for r, (f, g) in enumerate(rows):
            hi, lo = max(FEATURES[f], FEATURES[g]), min(FEATURES[f], FEATURES[g])
            w1p[r, c] = w1[D + hi * (hi - 1) // 2 + lo]
            packing[g % QUADS, f - 1, g // QUADS, r] = 1.0
    w1p[ONES_ROW, 0] = np.asarray(inputs["b_top1"])
    packing[G % QUADS, 0, G // QUADS, ONES_ROW] = 1.0
    w1b = np.stack([w1[:D], w1[D + PAIRS:]], axis=1)

    rows = 128 * HOT_CHUNKS
    hot = np.zeros((HOT, rows, D), np.float32)
    for i, f in enumerate(HOT_TABLES):
        hot[i, :VOCAB[f]] = np.asarray(inputs[f"tbl_{f}"])
    ids = np.asarray(inputs["ids"])

    args = [
        dram("bottom_dram", inputs["r_bottom_mlp_out"]),
        dram("ids_dram", ids[:, COLD_TABLES]),
        dram("hot_ids_dram", ids[:, HOT_TABLES].T),
        dram("hot_offsets_dram", -np.arange(rows, dtype=np.float32).reshape(128, HOT_CHUNKS)[:, :2]),
        dram("hot_tables_dram", hot.reshape(HOT, 128, HOT_CHUNKS, D)),
        [dram(f"tbl_{f}_dram", inputs[f"tbl_{f}"]) for f in COLD_TABLES],
        dram("packing_dram", packing.reshape(128, CHUNKS, 128)),
        dram("w1p_dram", w1p),
        dram("w1b_dram", w1b),
        dram("w2_dram", inputs["W_top2"]),
        dram("b2_dram", inputs["b_top2"]),
        dram("w3_dram", inputs["W_top3"]),
        nc.dram_tensor("y_dram", (B, 1), mybir.dt.float32, kind="ExternalOutput").ap(),
    ]
    build(nc, *args)
    r = run_bass_kernel_spmd(nc, [arrays], core_ids=[0])
    return r.results[0]["y_dram"]
```
